# Optimizing a Trainium2 kernel written in Bass

```python
import numpy as np
import jax
import jax.numpy as jnp

def _softmax(x, axis=-1):
    return jax.nn.softmax(x, axis=axis)

def _gelu(x):
    return jax.nn.gelu(x, approximate=True)

def _silu(x):
    return jax.nn.silu(x)

def _sigmoid(x):
    return jax.nn.sigmoid(x)

def _layernorm(x, axis=-1, eps=1e-05):
    m = jnp.mean(x, axis=axis, keepdims=True)
    v = jnp.var(x, axis=axis, keepdims=True)
    return (x - m) / jnp.sqrt(v + eps)

def _scatter_add(tgt, idx, src, axis=0):
    return tgt.at[idx].add(src)

def _segment_sum(src, seg, n):
    return jax.ops.segment_sum(src, seg, n)
kernel_name = 'mk_dlrm_tower_d1_rec_r8_c88e78'

def setup_inputs(seed: int=0):
    np.random.seed(seed)
    _w = jnp.asarray

    def _rec_inputs():
        import jax
        import jax.numpy as jnp
        _tk = jax.random.key(seed)
        ids = jnp.stack([jax.random.randint(jax.random.fold_in(_tk, 200 + f), (2048,), 0, v, jnp.int32) for f, v in enumerate([1250, 1000, 125000, 1250, 1250, 1250, 12500, 1000, 12500, 12500, 1250, 1000, 12500, 1250, 1250, 1250, 1000, 1250, 1000, 1000, 12500, 1000, 1250, 1000, 1250, 1000])], axis=1)
        tbl_0 = 0.05 * jax.random.normal(jax.random.fold_in(_tk, 500 + 0), (1250, 128), jnp.float32)
        tbl_1 = 0.05 * jax.random.normal(jax.random.fold_in(_tk, 500 + 1), (1000, 128), jnp.float32)
        tbl_2 = 0.05 * jax.random.normal(jax.random.fold_in(_tk, 500 + 2), (125000, 128), jnp.float32)
        tbl_3 = 0.05 * jax.random.normal(jax.random.fold_in(_tk, 500 + 3), (1250, 128), jnp.float32)
        tbl_4 = 0.05 * jax.random.normal(jax.random.fold_in(_tk, 500 + 4), (1250, 128), jnp.float32)
        tbl_5 = 0.05 * jax.random.normal(jax.random.fold_in(_tk, 500 + 5), (1250, 128), jnp.float32)
        tbl_6 = 0.05 * jax.random.normal(jax.random.fold_in(_tk, 500 + 6), (12500, 128), jnp.float32)
        tbl_7 = 0.05 * jax.random.normal(jax.random.fold_in(_tk, 500 + 7), (1000, 128), jnp.float32)
        tbl_8 = 0.05 * jax.random.normal(jax.random.fold_in(_tk, 500 + 8), (12500, 128), jnp.float32)
        tbl_9 = 0.05 * jax.random.normal(jax.random.fold_in(_tk, 500 + 9), (12500, 128), jnp.float32)
        tbl_10 = 0.05 * jax.random.normal(jax.random.fold_in(_tk, 500 + 10), (1250, 128), jnp.float32)
        tbl_11 = 0.05 * jax.random.normal(jax.random.fold_in(_tk, 500 + 11), (1000, 128), jnp.float32)
        tbl_12 = 0.05 * jax.random.normal(jax.random.fold_in(_tk, 500 + 12), (12500, 128), jnp.float32)
        tbl_13 = 0.05 * jax.random.normal(jax.random.fold_in(_tk, 500 + 13), (1250, 128), jnp.float32)
        tbl_14 = 0.05 * jax.random.normal(jax.random.fold_in(_tk, 500 + 14), (1250, 128), jnp.float32)
        tbl_15 = 0.05 * jax.random.normal(jax.random.fold_in(_tk, 500 + 15), (1250, 128), jnp.float32)
        tbl_16 = 0.05 * jax.random.normal(jax.random.fold_in(_tk, 500 + 16), (1000, 128), jnp.float32)
        tbl_17 = 0.05 * jax.random.normal(jax.random.fold_in(_tk, 500 + 17), (1250, 128), jnp.float32)
        tbl_18 = 0.05 * jax.random.normal(jax.random.fold_in(_tk, 500 + 18), (1000, 128), jnp.float32)
        tbl_19 = 0.05 * jax.random.normal(jax.random.fold_in(_tk, 500 + 19), (1000, 128), jnp.float32)
        tbl_20 = 0.05 * jax.random.normal(jax.random.fold_in(_tk, 500 + 20), (12500, 128), jnp.float32)
        tbl_21 = 0.05 * jax.random.normal(jax.random.fold_in(_tk, 500 + 21), (1000, 128), jnp.float32)
        tbl_22 = 0.05 * jax.random.normal(jax.random.fold_in(_tk, 500 + 22), (1250, 128), jnp.float32)
        tbl_23 = 0.05 * jax.random.normal(jax.random.fold_in(_tk, 500 + 23), (1000, 128), jnp.float32)
        tbl_24 = 0.05 * jax.random.normal(jax.random.fold_in(_tk, 500 + 24), (1250, 128), jnp.float32)
        tbl_25 = 0.05 * jax.random.normal(jax.random.fold_in(_tk, 500 + 25), (1000, 128), jnp.float32)
        _rk = jax.random.fold_in(_tk, 7)
        r_bottom_output = -0.000520686 + 1.00062 * jax.random.normal(jax.random.fold_in(_rk, 101), (2048, 128), jnp.float32)
        W_top1 = 0.0456912 * jax.random.normal(jax.random.fold_in(_tk, 801), (479, 512), jnp.float32)
        W_top2 = 0.0441942 * jax.random.normal(jax.random.fold_in(_tk, 802), (512, 256), jnp.float32)
        W_top3 = 0.0625 * jax.random.normal(jax.random.fold_in(_tk, 803), (256, 1), jnp.float32)
        b_top1 = jnp.zeros((512,), jnp.float32)
        b_top2 = jnp.zeros((256,), jnp.float32)
        return (r_bottom_output, ids, tbl_0, tbl_1, tbl_2, tbl_3, tbl_4, tbl_5, tbl_6, tbl_7, tbl_8, tbl_9, tbl_10, tbl_11, tbl_12, tbl_13, tbl_14, tbl_15, tbl_16, tbl_17, tbl_18, tbl_19, tbl_20, tbl_21, tbl_22, tbl_23, tbl_24, tbl_25, W_top1, b_top1, W_top2, b_top2, W_top3)
    r_bottom_output, ids, tbl_0, tbl_1, tbl_2, tbl_3, tbl_4, tbl_5, tbl_6, tbl_7, tbl_8, tbl_9, tbl_10, tbl_11, tbl_12, tbl_13, tbl_14, tbl_15, tbl_16, tbl_17, tbl_18, tbl_19, tbl_20, tbl_21, tbl_22, tbl_23, tbl_24, tbl_25, W_top1, b_top1, W_top2, b_top2, W_top3 = _rec_inputs()

    def _L0_rec_setup():
        import jax, jax.numpy as jnp
        import numpy as np
        NUM_FEATURES = 27
        _TRIU_I, _TRIU_J = np.triu_indices(NUM_FEATURES, k=1)
        key = jax.random.key(seed)
        k1, k2 = jax.random.split(key)
        bottom_output = jax.random.normal(k1, (2048, 128), dtype=jnp.float32)
        embeddings = jax.random.normal(k2, (2048, 26, 128), dtype=jnp.float32)
        return {'bottom_output': bottom_output, 'embeddings': embeddings}
    _L0_rec_all = _L0_rec_setup()
    _L0_rec_in = {k: v for k, v in _L0_rec_all.items() if k in ()}
    del _L0_rec_all
    return {'r_bottom_output': r_bottom_output, 'ids': ids, 'tbl_0': tbl_0, 'tbl_1': tbl_1, 'tbl_2': tbl_2, 'tbl_3': tbl_3, 'tbl_4': tbl_4, 'tbl_5': tbl_5, 'tbl_6': tbl_6, 'tbl_7': tbl_7, 'tbl_8': tbl_8, 'tbl_9': tbl_9, 'tbl_10': tbl_10, 'tbl_11': tbl_11, 'tbl_12': tbl_12, 'tbl_13': tbl_13, 'tbl_14': tbl_14, 'tbl_15': tbl_15, 'tbl_16': tbl_16, 'tbl_17': tbl_17, 'tbl_18': tbl_18, 'tbl_19': tbl_19, 'tbl_20': tbl_20, 'tbl_21': tbl_21, 'tbl_22': tbl_22, 'tbl_23': tbl_23, 'tbl_24': tbl_24, 'tbl_25': tbl_25, 'W_top1': W_top1, 'b_top1': b_top1, 'W_top2': W_top2, 'b_top2': b_top2, 'W_top3': W_top3}

def reference(r_bottom_output, ids, tbl_0, tbl_1, tbl_2, tbl_3, tbl_4, tbl_5, tbl_6, tbl_7, tbl_8, tbl_9, tbl_10, tbl_11, tbl_12, tbl_13, tbl_14, tbl_15, tbl_16, tbl_17, tbl_18, tbl_19, tbl_20, tbl_21, tbl_22, tbl_23, tbl_24, tbl_25, W_top1, b_top1, W_top2, b_top2, W_top3):
    import jax
    import jax.numpy as jnp

    def _L0_rec_ref(bottom_output, embeddings):
        import jax, jax.numpy as jnp
        import numpy as np
        NUM_FEATURES = 27
        _TRIU_I, _TRIU_J = np.triu_indices(NUM_FEATURES, k=1)
        all_emb = jnp.concatenate([bottom_output[:, None, :], embeddings], axis=1)
        gram = jnp.einsum('bfd,bgd->bfg', all_emb, all_emb)
        return gram[:, _TRIU_I, _TRIU_J]
    e = jnp.stack([tbl_0[ids[:, 0]], tbl_1[ids[:, 1]], tbl_2[ids[:, 2]], tbl_3[ids[:, 3]], tbl_4[ids[:, 4]], tbl_5[ids[:, 5]], tbl_6[ids[:, 6]], tbl_7[ids[:, 7]], tbl_8[ids[:, 8]], tbl_9[ids[:, 9]], tbl_10[ids[:, 10]], tbl_11[ids[:, 11]], tbl_12[ids[:, 12]], tbl_13[ids[:, 13]], tbl_14[ids[:, 14]], tbl_15[ids[:, 15]], tbl_16[ids[:, 16]], tbl_17[ids[:, 17]], tbl_18[ids[:, 18]], tbl_19[ids[:, 19]], tbl_20[ids[:, 20]], tbl_21[ids[:, 21]], tbl_22[ids[:, 22]], tbl_23[ids[:, 23]], tbl_24[ids[:, 24]], tbl_25[ids[:, 25]]], axis=1)
    z = _L0_rec_ref(r_bottom_output, e)
    z = z.reshape(z.shape[0], -1)
    h = jnp.concatenate([z, r_bottom_output], axis=1)
    h = jnp.maximum(h @ W_top1 + b_top1, 0.0)
    h = jnp.maximum(h @ W_top2 + b_top2, 0.0)
    y = h @ W_top3
    return y

_drawn_inputs = setup_inputs


def setup_inputs(seed=0):
    import zlib

    import numpy as np

    out = dict(_drawn_inputs(seed))
    spreads = {'b_top1': (0.0, 0.1), 'b_top2': (0.0, 0.1)}
    factors = {}
    for name, (base, spread) in spreads.items():
        noise = np.random.default_rng([zlib.crc32(name.encode()), seed]).standard_normal(out[name].shape)
        drawn = base * np.exp(spread * noise) if base else spread * noise
        out[name] = jnp.asarray(drawn.astype(out[name].dtype))
    for name, factor in factors.items():
        out[name] = (out[name] * factor).astype(out[name].dtype)
    return out
```

```python
from contextlib import ExitStack

import numpy as np

import concourse.bass as bass
from concourse import mybir

ACT = mybir.ActivationFunctionType
ALU = mybir.AluOpType
F32 = mybir.dt.float32
I32 = mybir.dt.int32

P = 128
NUM_TABLES = 26
F = NUM_TABLES + 1
GROUP = 4
GROUPS = [list(range(a, min(a + GROUP, F))) for a in range(1, F, GROUP)]
NG = len(GROUPS)
QUAD = 32
NQUAD = P // QUAD
HALVES = 2
PER_QUAD = P // HALVES // NQUAD
PAIR = 2 * P


def pair_rows():
    pieces, row = [], 0
    for f in range(F - 1):
        g = f + 1
        while g < F:
            n = min(F - g, P - row % P)
            pieces.append((f, g, row // P, row % P, n))
            g += n
            row += n
    return pieces, row


PIECES, NPAIRS = pair_rows()
ZCHUNKS = -(-NPAIRS // P)


def tower(nc, bottomT, ids, tables, W1, b1, W2, b2, W3, out):
    B = bottomT.shape[1]
    TILES = B // P
    NPAIR_TILES = B // PAIR
    H1, H2 = W1.shape[1], W2.shape[1]
    M1, M2 = H1 // P, H2 // P
    chunk_rows = [min(P, NPAIRS - P * c) for c in range(ZCHUNKS)] + [P]
    chunk_first = [P * c for c in range(ZCHUNKS)] + [NPAIRS]
    PACKED = 16 * len(PIECES)

    with ExitStack() as ctx:
        def sb(name, shape, dt=F32):
            return ctx.enter_context(nc.sbuf_tensor(name, shape, dt))

        def sem(name):
            return ctx.enter_context(nc.semaphore(name))

        identity = sb("identity", [P, P])
        ids_all = sb("ids_all", [P, TILES + 1, NUM_TABLES], I32)
        ids_now = [sb(f"ids_now{p}", [P, NUM_TABLES], I32) for p in range(2)]
        rows = [sb(f"rows{p}", [P, F, P]) for p in range(2)]
        embT = [sb(f"embT{p}", [P, P, F]) for p in range(2)]
        bottom = sb("bottom", [P, B])
        gram = sb("gram", [F, F, PAIR])
        z = sb("z", [P, ZCHUNKS, PAIR])
        w1 = sb("w1", [P, ZCHUNKS + 1, H1])
        w2 = sb("w2", [P, M1, H2])
        w3 = sb("w3", [P, M2])
        bias1 = sb("bias1", [P, M1])
        bias2 = sb("bias2", [P, M2])
        h1 = sb("h1", [P, M1, PAIR])
        h2 = sb("h2", [P, M2, PAIR])
        y = sb("y", [1, PAIR])

        turned = [ctx.enter_context(nc.psum_tensor(f"turned{b}", [P, GROUP, P], F32)) for b in range(2)]
        gram_ps = [ctx.enter_context(nc.psum_tensor(f"gram_ps{h}", [P, PER_QUAD, F], F32)) for h in range(HALVES)]
        h1_ps = [ctx.enter_context(nc.psum_tensor(f"h1_ps{b}", [P, 512], F32)) for b in range(2)]
        h2_ps = [ctx.enter_context(nc.psum_tensor(f"h2_ps{b}", [P, 512], F32)) for b in range(2)]
        y_ps = h1_ps[0][0:1, 0:PAIR]

        ids_loaded = sem("ids_loaded")
        bottom_loaded = sem("bottom_loaded")
        weights_loaded = sem("weights_loaded")
        identity_zero = sem("identity_zero")
        identity_ready = sem("identity_ready")
        pad_ready = sem("pad_ready")
        ids_staged = sem("ids_staged")
        tile_begun = sem("tile_begun")
        gathered = [[sem(f"gathered{p}_{g}") for g in range(NG)] for p in range(2)]
        group_turned = sem("group_turned")
        group_placed = sem("group_placed")
        bottom_placed = sem("bottom_placed")
        gram_done = sem("gram_done")
        gram_moved = sem("gram_moved")
        z_packed = sem("z_packed")
        h1_done = sem("h1_done")
        h1_ready = sem("h1_ready")
        h2_done = sem("h2_done")
        h2_ready = sem("h2_ready")
        y_done = sem("y_done")
        y_ready = sem("y_ready")
        y_stored = sem("y_stored")

        WEIGHT_LOADS = len(chunk_rows) + 4
        block = ctx.enter_context(nc.Block())

        @block.sync
        def _(sp):
            sp.dma_start(ids_all[:, 0:TILES, :], ids.rearrange("(t p) f -> p t f", p=P)).then_inc(ids_loaded, 16)
            sp.dma_start(bottom[:], bottomT).then_inc(bottom_loaded, 16)

            def pack(i, first):
                if not first:
                    sp.wait_ge(h1_done, M1 * i)
                    sp.wait_ge(ids_loaded, 16)
                sp.wait_ge(gram_moved, 2 * HALVES * (i + 1))
                for f, g, chunk, row, n in PIECES:
                    sp.dma_start(z[row:row + n, chunk, :], gram[g:g + n, f, :]).then_inc(z_packed, 16)

            pack(0, True)
            with sp.Fori(1, NPAIR_TILES) as i:
                pack(i, False)

        @block.gpsimd
        def _(pool):
            pool.memset(identity[:], 0.0).then_inc(identity_zero, 1)
            pool.wait_ge(identity_zero, 1)
            pool.affine_select(out=identity[:], in_=identity[:], compare_op=ALU.not_equal, fill=1.0, base=0,
                               pattern=[[-1, P]], channel_multiplier=1).then_inc(identity_ready, 1)

            def gather(i, p, first):
                if not first:
                    pool.wait_ge(group_turned, NG * (2 * i + p - 1))
                pool.wait_ge(ids_staged, 2 * i + p + 1)
                pool.sem_inc(tile_begun, 1)
                for g, features in enumerate(GROUPS):
                    for f in features:
                        pool.indirect_dma_start(
                            rows[p][:, f, :], None, tables[f - 1],
                            bass.IndirectOffsetOnAxis(ap=ids_now[p][:, f - 1:f], axis=0),
                        ).then_inc(gathered[p][g], 16)

            for p in range(2):
                gather(0, p, True)
            with pool.Fori(1, NPAIR_TILES) as i:
                for p in range(2):
                    gather(i, p, False)

        @block.tensor
        def _(pe):
            def turn(i, p, first):
                for g, features in enumerate(GROUPS):
                    b = (NG * p + g) % 2
                    pe.wait_ge(gathered[p][g], 16 * len(features) * (i + 1))
                    if not (first and NG * p + g < 2):
                        pe.wait_ge(group_placed, NG * (2 * i + p) + g - 1)
                    for k, f in enumerate(features):
                        mm = pe.transpose(turned[b][:, k, :], rows[p][:, f, :], identity[:])
                    mm.then_inc(group_turned, 1)

            def grams(i, p, first):
                pe.wait_ge(group_placed, NG * (2 * i + p + 1))
                pe.wait_ge(bottom_placed, 2 * i + p + 1)
                for h in range(HALVES):
                    if not (first and p == 0):
                        pe.wait_ge(gram_moved, HALVES * (2 * i + p - 1) + h + 1)
                    for q in range(PER_QUAD):
                        for c in range(NQUAD):
                            e = embT[p][:, (h * NQUAD + c) * PER_QUAD + q, :]
                            mm = pe.matmul(gram_ps[h][QUAD * c:QUAD * c + F, q, :], e, e, start=True, stop=True)
                    mm.then_inc(gram_done, 1)

            def mlp(j, first):
                pe.wait_ge(z_packed, PACKED * (j + 1))
                for m in range(M1):
                    if m == 0 and not first:
                        pe.wait_ge(y_ready, j)
                    if m >= 2:
                        pe.wait_ge(h1_ready, M1 * j + m - 1)
                    for k, n in enumerate(chunk_rows):
                        x = z[0:n, k, :] if k < ZCHUNKS else bottom[:, bass.ds(PAIR * j, PAIR)]
                        mm = pe.matmul(h1_ps[m % 2][:, 0:PAIR], w1[0:n, k, P * m:P * m + P], x,
                                       start=(k == 0), stop=(k == ZCHUNKS))
                    mm.then_inc(h1_done, 1)
                for m in range(M2):
                    for k in range(M1):
                        if m == 0:
                            pe.wait_ge(h1_ready, M1 * j + k + 1)
                        mm = pe.matmul(h2_ps[m % 2][:, 0:PAIR], w2[:, k, P * m:P * m + P], h1[:, k, :],
                                       start=(k == 0), stop=(k == M1 - 1))
                    mm.then_inc(h2_done, 1)
                for k in range(M2):
                    pe.wait_ge(h2_ready, M2 * j + k + 1)
                    mm = pe.matmul(y_ps, w3[:, k:k + 1], h2[:, k, :], start=(k == 0), stop=(k == M2 - 1))
                mm.then_inc(y_done, 1)

            pe.wait_ge(identity_ready, 1)
            for p in range(2):
                turn(0, p, True)
                grams(0, p, True)
            pe.wait_ge(weights_loaded, 16 * WEIGHT_LOADS)
            pe.wait_ge(bottom_loaded, 16)
            turn(1, 0, False)
            grams(1, 0, False)
            mlp(0, True)
            turn(1, 1, False)
            grams(1, 1, False)
            with pe.Fori(2, NPAIR_TILES) as i:
                turn(i, 0, False)
                grams(i, 0, False)
                mlp(i - 1, False)
                turn(i, 1, False)
                grams(i, 1, False)
            mlp(NPAIR_TILES - 1, False)

        @block.vector
        def _(dve):
            def stage_ids(t, slot):
                dve.tensor_copy(ids_now[slot][:], ids_all[:, bass.ds(t, 1), :].rearrange("p a f -> p (a f)")).then_inc(ids_staged, 1)

            def place(i, p, first):
                if not first:
                    dve.wait_ge(gram_done, HALVES * (2 * i + p - 1))
                dve.tensor_copy(embT[p][:, :, 0], bottom[:, bass.ds(P * (2 * i + p), P)]).then_inc(bottom_placed, 1)
                for g, features in enumerate(GROUPS):
                    n = len(features)
                    dve.wait_ge(group_turned, NG * (2 * i + p) + g + 1)
                    dve.tensor_copy(embT[p][:, :, features[0]:features[0] + n],
                                    turned[(NG * p + g) % 2][:, 0:n, :].rearrange("p f s -> p s f"),
                                    ).then_inc(group_placed, 1)

            dve.memset(ids_all[:, TILES, :], 0).then_inc(pad_ready, 1)
            dve.wait_ge(ids_loaded, 16)
            stage_ids(0, 0)
            dve.wait_ge(bottom_loaded, 16)
            dve.wait_ge(pad_ready, 1)
            stage_ids(1, 1)
            place(0, 0, True)
            stage_ids(2, 0)
            place(0, 1, True)
            with dve.Fori(1, NPAIR_TILES) as i:
                stage_ids(2 * i + 1, 1)
                place(i, 0, False)
                stage_ids(2 * i + 2, 0)
                place(i, 1, False)

        @block.scalar
        def _(act):
            for k, n in enumerate(chunk_rows):
                act.dma_start(w1[0:n, k, :], W1[chunk_first[k]:chunk_first[k] + n, :]).then_inc(weights_loaded, 16)
            act.dma_start(w2[:], W2.rearrange("(k p) n -> p k n", p=P)).then_inc(weights_loaded, 16)
            for tile, dram in ((w3, W3), (bias1, b1), (bias2, b2)):
                act.dma_start(tile[:], dram).then_inc(weights_loaded, 16)

            def move_gram(i, p, first):
                if p == 0 and not first:
                    act.wait_ge(z_packed, PACKED * i)
                for h in range(HALVES):
                    act.wait_ge(gram_done, HALVES * (2 * i + p) + h + 1)
                    for c in range(NQUAD):
                        s = P * p + (h * NQUAD + c) * PER_QUAD
                        ins = act.copy(gram[:, :, s:s + PER_QUAD],
                                       gram_ps[h][QUAD * c:QUAD * c + F, :, :].rearrange("f s g -> f g s"))
                    ins.then_inc(gram_moved, 1)

            def mlp(j, first):
                for m in range(M1):
                    act.wait_ge(h1_done, M1 * j + m + 1)
                    if m == 0 and not first:
                        act.wait_ge(h2_done, M2 * j)
                    act.activation(h1[:, m, :], h1_ps[m % 2][:, 0:PAIR], ACT.Relu, bias=bias1[:, m:m + 1]).then_inc(h1_ready, 1)
                for m in range(M2):
                    act.wait_ge(h2_done, M2 * j + m + 1)
                    if m == 0 and not first:
                        act.wait_ge(y_done, j)
                    act.activation(h2[:, m, :], h2_ps[m % 2][:, 0:PAIR], ACT.Relu, bias=bias2[:, m:m + 1]).then_inc(h2_ready, 1)
                act.wait_ge(y_done, j + 1)
                if not first:
                    act.wait_ge(y_stored, 16 * j)
                act.copy(y[:], y_ps).then_inc(y_ready, 1)
                act.wait_ge(y_ready, j + 1)
                act.dma_start(out[:, bass.ds(PAIR * j, PAIR)], y[:]).then_inc(y_stored, 16)

            for p in range(2):
                move_gram(0, p, True)
            act.wait_ge(weights_loaded, 16 * WEIGHT_LOADS)
            move_gram(1, 0, False)
            mlp(0, True)
            move_gram(1, 1, False)
            with act.Fori(2, NPAIR_TILES) as i:
                move_gram(i, 0, False)
                mlp(i - 1, False)
                move_gram(i, 1, False)
            mlp(NPAIR_TILES - 1, False)
            act.wait_ge(y_stored, 16 * NPAIR_TILES)


def kernel(**inputs):
    import concourse.bacc as bacc
    from concourse.bass_utils import run_bass_kernel_spmd

    nc = bacc.Bacc("TRN2", target_bir_lowering=False, num_devices=1)
    arrays = {}

    def dram(name, a):
        arrays[name] = np.ascontiguousarray(a)
        return nc.dram_tensor(name, arrays[name].shape, mybir.dt.from_np(arrays[name].dtype), kind="ExternalInput").ap()

    bottomT = dram("bottomT", np.asarray(inputs["r_bottom_output"]).T)
    ids = dram("ids", inputs["ids"])
    tables = [dram(f"tbl_{n}", inputs[f"tbl_{n}"]) for n in range(NUM_TABLES)]
    W1 = dram("W1", inputs["W_top1"])
    b1 = dram("b1", np.asarray(inputs["b_top1"]).reshape(-1, P).T)
    W2 = dram("W2", inputs["W_top2"])
    b2 = dram("b2", np.asarray(inputs["b_top2"]).reshape(-1, P).T)
    W3 = dram("W3", np.asarray(inputs["W_top3"]).reshape(-1, P).T)
    B = arrays["ids"].shape[0]
    out = nc.dram_tensor("out", (1, B), F32, kind="ExternalOutput").ap()
    tower(nc, bottomT, ids, tables, W1, b1, W2, b2, W3, out)
    r = run_bass_kernel_spmd(nc, [arrays], core_ids=[0])
    return np.asarray(r.results[0]["out"]).reshape(B, 1)
```

```python
from contextlib import ExitStack

import numpy as np

import concourse.bass as bass
from concourse import mybir

ACT = mybir.ActivationFunctionType
ALU = mybir.AluOpType
F32 = mybir.dt.float32
BF16 = mybir.dt.bfloat16
I32 = mybir.dt.int32

P = 128
NUM_TABLES = 26
F = NUM_TABLES + 1
LOOKED_UP = (20, 22, 24, 26)
GATHERED = [f for f in range(1, F) if f not in LOOKED_UP]
GROUP = 4
PARTS = 3


def evenly_spaced(features, most):
    runs = []
    for f in features:
        run = runs[-1] if runs else []
        if run and len(run) < most and (len(run) == 1 or f - run[-1] == run[-1] - run[-2]):
            run.append(f)
        else:
            runs.append([f])
    return runs


GROUPS = evenly_spaced(GATHERED, GROUP)
NG = len(GROUPS)
NL = len(LOOKED_UP)
QUAD = 32
NQUAD = P // QUAD
HALVES = 2
PER_QUAD = P // HALVES // NQUAD
PAIR = 2 * P


CHUNKS = 3

TRIPLES = []
ZROWS = 0
for t in range(0, F - 1, CHUNKS):
    TRIPLES.append((t, t + 1, ZROWS, F - 1 - t))
    ZROWS += F - 1 - t
assert ZROWS <= P


def tower(nc, bottomT, ids, ids_rows, tables, W1, b1, W2, b2, W3, out):
    B = bottomT.shape[1]
    TILES = B // P
    NPAIR_TILES = B // PAIR
    H1, H2 = W1.shape[1], W2.shape[1]
    M1, M2 = H1 // P, H2 // P
    chunk_rows = [ZROWS] * CHUNKS + [P]
    NPAIRS = F * (F - 1) // 2
    V = tables[LOOKED_UP[0] - 1].shape[0]
    VCHUNKS = -(-V // P)
    VROWS = V // VCHUNKS
    assert VROWS * VCHUNKS == V and all(tables[f - 1].shape[0] == V for f in LOOKED_UP)
    PACKED = 16 * len(TRIPLES)

    with ExitStack() as ctx:
        def sb(name, shape, dt=F32):
            return ctx.enter_context(nc.sbuf_tensor(name, shape, dt))

        def sem(name):
            return ctx.enter_context(nc.semaphore(name))

        identity = sb("identity", [P, P])
        ids_all = sb("ids_all", [P, TILES + 1, NUM_TABLES], I32)
        ids_now = [sb(f"ids_now{p}", [P, NUM_TABLES], I32) for p in range(2)]
        rows = [sb(f"rows{p}", [P, F, P]) for p in range(2)]
        embT = sb("embT", [P, PAIR, F])
        row_number_i = sb("row_number_i", [P, VCHUNKS], I32)
        row_number = sb("row_number", [P, VCHUNKS])
        ids_wide = sb("ids_wide", [P, NL, B], I32)
        onehot = [sb(f"onehot{b}", [P, VCHUNKS, PAIR], BF16) for b in range(2)]
        parts = sb("parts", [P, NL, PARTS, VCHUNKS, P], BF16)
        bottom = sb("bottom", [P, B])
        gram = sb("gram", [P, F, PAIR])
        small = gram[0:VROWS].rearrange("p f s -> p (f s)")[:, 0:NL * VCHUNKS * P].rearrange(
            "p (n c d) -> p n c d", n=NL, c=VCHUNKS)
        z = sb("z", [P, CHUNKS, PAIR])
        w1 = sb("w1", [P, CHUNKS + 1, H1])
        w2 = sb("w2", [P, M1, H2])
        w3 = sb("w3", [P, M2])
        bias1 = sb("bias1", [P, M1])
        bias2 = sb("bias2", [P, M2])
        h1 = sb("h1", [P, M1, PAIR])
        h2 = sb("h2", [P, M2, PAIR])
        y = sb("y", [1, PAIR])

        turned = [ctx.enter_context(nc.psum_tensor(f"turned{b}", [P, GROUP, P], F32)) for b in range(2)]
        gram_ps = [ctx.enter_context(nc.psum_tensor(f"gram_ps{h}", [P, PER_QUAD, F], F32)) for h in range(HALVES)]
        looked_ps = [ctx.enter_context(nc.psum_tensor(f"looked_ps{b}", [P, 512], F32)) for b in range(2)]
        mlp_ps = [ctx.enter_context(nc.psum_tensor(f"mlp_ps{b}", [P, 512], F32)) for b in range(2)]
        y_ps = mlp_ps[0][0:1, 0:PAIR]

        ids_loaded = sem("ids_loaded")
        bottom_loaded = sem("bottom_loaded")
        weights_loaded = sem("weights_loaded")
        identity_zero = sem("identity_zero")
        identity_ready = sem("identity_ready")
        pad_ready = sem("pad_ready")
        ids_staged = sem("ids_staged")
        tile_begun = sem("tile_begun")
        gathered = [[sem(f"gathered{p}_{g}") for g in range(NG)] for p in range(2)]
        group_turned = sem("group_turned")
        group_placed = sem("group_placed")
        bottom_placed = sem("bottom_placed")
        wide_loaded = sem("wide_loaded")
        rest_loaded = sem("rest_loaded")
        numbers_made = sem("numbers_made")
        numbers_ready = sem("numbers_ready")
        small_loaded = [sem(f"small_loaded{n}") for n in range(NL)]
        part_cast = [sem(f"part_cast{k}") for k in range(PARTS)]
        rest_left = [sem(f"rest_left{k}") for k in range(PARTS - 1)]
        onehot_built = sem("onehot_built")
        looked_up = sem("looked_up")
        lookup_placed = sem("lookup_placed")
        w1_zero = sem("w1_zero")
        gram_done = sem("gram_done")
        gram_moved = sem("gram_moved")
        z_packed = sem("z_packed")
        h1_done = sem("h1_done")
        h1_ready = sem("h1_ready")
        h2_done = sem("h2_done")
        h2_ready = sem("h2_ready")
        y_done = sem("y_done")
        y_ready = sem("y_ready")
        y_stored = sem("y_stored")

        WEIGHT_LOADS = F - 1 + 1 + 4
        LAST = NPAIR_TILES - 1

        def uses_before(i, n):
            if n >= 2:
                return NL * i + n - 1
            return NL * i - (NL - n) % 2
        block = ctx.enter_context(nc.Block())

        @block.sync
        def _(sp):
            sp.dma_start(ids_all[:, 0:TILES, :], ids.rearrange("(t p) f -> p t f", p=P)).then_inc(ids_loaded, 16)
            for n in range(NL):
                sp.dma_start(ids_wide[:, n, 0:PAIR], ids_rows[n:n + 1, 0:PAIR].to_broadcast([P, PAIR])).then_inc(wide_loaded, 16)
            sp.dma_start(bottom[:], bottomT).then_inc(bottom_loaded, 16)
            sp.wait_ge(w1_zero, 1)
            w1_row = 0
            for f in range(F - 1):
                first_f, first_g, row, n = TRIPLES[f // CHUNKS]
                row += f + 1 - first_g
                n = F - 1 - f
                sp.dma_start(w1[row:row + n, f - first_f, :], W1[w1_row:w1_row + n, :]).then_inc(weights_loaded, 16)
                w1_row += n
            sp.dma_start(w1[:, CHUNKS, :], W1[NPAIRS:NPAIRS + P, :]).then_inc(weights_loaded, 16)

            for n in range(NL):
                sp.dma_start(ids_wide[:, n, PAIR:B], ids_rows[n:n + 1, PAIR:B].to_broadcast([P, B - PAIR])).then_inc(rest_loaded, 16)

            def pack(b, moved, at=0, width=PAIR, first=False):
                if not first:
                    sp.wait_ge(h1_done, M1 * b)
                sp.wait_ge(gram_moved, HALVES * moved)
                for f, g, row, n in TRIPLES:
                    sp.dma_start(z[row:row + n, :, at:at + width],
                                 gram[g:g + n, f:f + CHUNKS, at:at + width]).then_inc(z_packed, 16)

            pack(0, 2, first=True)
            with sp.Fori(1, LAST) as i:
                pack(i, 2 * i + 2)
            pack(LAST, TILES - 1, 0, P)
            pack(LAST + 1, TILES, P, P)

        @block.gpsimd
        def _(pool):
            pool.memset(identity[:], 0.0).then_inc(identity_zero, 1)
            pool.wait_ge(identity_zero, 1)
            pool.affine_select(out=identity[:], in_=identity[:], compare_op=ALU.not_equal, fill=1.0, base=0,
                               pattern=[[-1, P]], channel_multiplier=1).then_inc(identity_ready, 1)

            pool.iota(row_number_i[:], pattern=[[VROWS, VCHUNKS]], base=0, channel_multiplier=1).then_inc(numbers_made, 1)

            def gather(i, p, first):
                if not first:
                    pool.wait_ge(group_turned, NG * (2 * i + p - 1))
                pool.wait_ge(ids_staged, 2 * i + p + 1)
                pool.sem_inc(tile_begun, 1)
                for g, features in enumerate(GROUPS):
                    for f in features:
                        pool.indirect_dma_start(
                            rows[p][:, f, :], None, tables[f - 1],
                            bass.IndirectOffsetOnAxis(ap=ids_now[p][:, f - 1:f], axis=0),
                        ).then_inc(gathered[p][g], 16)

            for p in range(2):
                gather(0, p, True)
            with pool.Fori(1, NPAIR_TILES) as i:
                for p in range(2):
                    gather(i, p, False)

        @block.tensor
        def _(pe):
            def look_up(i, first):
                for n in range(NL):
                    if first:
                        pe.wait_ge(part_cast[PARTS - 1], n + 1)
                    pe.wait_ge(onehot_built, NL * i + n + 1)
                    if not (first and n < 2):
                        pe.wait_ge(lookup_placed, uses_before(i, n))
                    for c in range(VCHUNKS):
                        for part in range(PARTS):
                            mm = pe.matmul(looked_ps[n % 2][:, 0:PAIR], parts[0:VROWS, n, part, c, :],
                                           onehot[n % 2][0:VROWS, c, :], start=(c == 0 and part == 0),
                                           stop=(c == VCHUNKS - 1 and part == PARTS - 1))
                    mm.then_inc(looked_up, 1)

            def turn(i, p, first):
                for g, features in enumerate(GROUPS):
                    b = (NG * p + g) % 2
                    pe.wait_ge(gathered[p][g], 16 * len(features) * (i + 1))
                    if not (first and NG * p + g < 2):
                        pe.wait_ge(group_placed, NG * (2 * i + p) + g - 1)
                    for k, f in enumerate(features):
                        mm = pe.transpose(turned[b][:, k, :], rows[p][:, f, :], identity[:])
                    mm.then_inc(group_turned, 1)

            def grams(i, p, first):
                pe.wait_ge(group_placed, NG * (2 * i + p + 1))
                pe.wait_ge(bottom_placed, i + 1)
                pe.wait_ge(lookup_placed, NL * (i + 1))
                for h in range(HALVES):
                    if not (first and p == 0):
                        pe.wait_ge(gram_moved, HALVES * (2 * i + p - 1) + h + 1)
                    for q in range(PER_QUAD):
                        for c in range(NQUAD):
                            e = embT[:, P * p + (h * NQUAD + c) * PER_QUAD + q, :]
                            mm = pe.matmul(gram_ps[h][QUAD * c:QUAD * c + F, q, :], e, e, start=True, stop=True)
                    mm.then_inc(gram_done, 1)

            def mlp(j, column, width=PAIR, at=0, first=False):
                pe.wait_ge(z_packed, PACKED * (j + 1))
                for m in range(M1):
                    if m == 0 and not first:
                        pe.wait_ge(y_ready, j)
                    if m >= 2:
                        pe.wait_ge(h1_ready, M1 * j + m - 1)
                    for k, n in enumerate(chunk_rows):
                        x = z[0:n, k, at:at + width] if k < CHUNKS else bottom[:, bass.ds(column, width)]
                        mm = pe.matmul(mlp_ps[m % 2][:, 0:width], w1[0:n, k, P * m:P * m + P], x,
                                       start=(k == 0), stop=(k == CHUNKS))
                    mm.then_inc(h1_done, 1)
                for m in range(M2):
                    for k in range(M1):
                        if m == 0:
                            pe.wait_ge(h1_ready, M1 * j + max(k + 1, M1 - 1))
                        mm = pe.matmul(mlp_ps[m % 2][:, 0:width], w2[:, k, P * m:P * m + P], h1[:, k, 0:width],
                                       start=(k == 0), stop=(k == M1 - 1))
                    mm.then_inc(h2_done, 1)
                for k in range(M2):
                    pe.wait_ge(h2_ready, M2 * j + k + 1)
                    mm = pe.matmul(y_ps[:, 0:width], w3[:, k:k + 1], h2[:, k, 0:width], start=(k == 0), stop=(k == M2 - 1))
                mm.then_inc(y_done, 1)

            pe.wait_ge(identity_ready, 1)
            look_up(0, True)
            for p in range(2):
                turn(0, p, True)
                grams(0, p, True)
            pe.wait_ge(weights_loaded, 16 * WEIGHT_LOADS)
            pe.wait_ge(bottom_loaded, 16)
            look_up(1, False)
            turn(1, 0, False)
            grams(1, 0, False)
            mlp(0, 0, first=True)
            turn(1, 1, False)
            grams(1, 1, False)
            with pe.Fori(2, LAST) as i:
                look_up(i, False)
                turn(i, 0, False)
                grams(i, 0, False)
                mlp(i - 1, PAIR * (i - 1))
                turn(i, 1, False)
                grams(i, 1, False)
            look_up(LAST, False)
            turn(LAST, 0, False)
            grams(LAST, 0, False)
            mlp(LAST - 1, PAIR * (LAST - 1))
            mlp(LAST, B - PAIR, P, 0)
            turn(LAST, 1, False)
            grams(LAST, 1, False)
            mlp(LAST + 1, B - P, P, P)

        @block.vector
        def _(dve):
            def stage_ids(t, slot):
                dve.tensor_copy(ids_now[slot][:], ids_all[:, bass.ds(t, 1), :].rearrange("p a f -> p (a f)")).then_inc(ids_staged, 1)

            def build_onehot(i, n, first):
                if not (first and n < 2):
                    dve.wait_ge(looked_up, uses_before(i, n))
                for c in range(VCHUNKS):
                    ins = dve.tensor_scalar(onehot[n % 2][:, c, :], ids_wide[:, n, bass.ds(PAIR * i, PAIR)],
                                            row_number[:, c:c + 1], None, ALU.is_equal)
                ins.then_inc(onehot_built, 1)

            def place_bottom(i, first):
                if not first:
                    dve.wait_ge(gram_done, 2 * HALVES * i)
                dve.tensor_copy(embT[:, :, 0], bottom[:, bass.ds(PAIR * i, PAIR)]).then_inc(bottom_placed, 1)

            def place(i, p, first):
                if not first:
                    dve.wait_ge(gram_done, HALVES * (2 * i + p - 1))
                for g, features in enumerate(GROUPS):
                    n = len(features)
                    step = features[1] - features[0] if n > 1 else 1
                    dve.wait_ge(group_turned, NG * (2 * i + p) + g + 1)
                    dve.tensor_copy(embT[:, P * p:P * p + P, features[0]:features[-1] + 1:step],
                                    turned[(NG * p + g) % 2][:, 0:n, :].rearrange("p f s -> p s f"),
                                    ).then_inc(group_placed, 1)

            def subtract_part(n, part):
                dve.wait_ge(part_cast[part], n + 1)
                dve.tensor_tensor(small[:, n], small[:, n], parts[0:VROWS, n, part], ALU.subtract
                                  ).then_inc(rest_left[part], 1)

            dve.memset(ids_all[:, TILES, :], 0).then_inc(pad_ready, 1)
            dve.wait_ge(ids_loaded, 16)
            stage_ids(0, 0)
            dve.wait_ge(pad_ready, 1)
            stage_ids(1, 1)
            dve.wait_ge(numbers_made, 1)
            dve.tensor_copy(row_number[:], row_number_i[:]).then_inc(numbers_ready, 1)
            dve.memset(w1[:], 0.0).then_inc(w1_zero, 1)

            subtract_part(0, 0)
            dve.wait_ge(numbers_ready, 1)
            dve.wait_ge(wide_loaded, 16 * NL)
            for n in range(NL):
                if n + 1 < NL:
                    subtract_part(n + 1, 0)
                build_onehot(0, n, True)
                subtract_part(n, 1)
            dve.wait_ge(bottom_loaded, 16)
            place_bottom(0, True)
            place(0, 0, True)
            stage_ids(2, 0)
            place(0, 1, True)
            dve.wait_ge(rest_loaded, 16 * NL)
            with dve.Fori(1, NPAIR_TILES) as i:
                stage_ids(2 * i + 1, 1)
                for n in range(NL):
                    build_onehot(i, n, False)
                place_bottom(i, False)
                place(i, 0, False)
                stage_ids(2 * i + 2, 0)
                place(i, 1, False)

        @block.scalar
        def _(act):
            def place_lookup(i, n):
                act.wait_ge(looked_up, NL * i + n + 1)
                act.copy(embT[:, :, LOOKED_UP[n]], looked_ps[n % 2][:, 0:PAIR]).then_inc(lookup_placed, 1)

            def place_lookups(i):
                act.wait_ge(gram_done, 2 * HALVES * i)
                for n in range(NL):
                    place_lookup(i, n)

            def cast_part(n, part):
                if part == 0:
                    act.wait_ge(small_loaded[n], 16)
                else:
                    act.wait_ge(rest_left[part - 1], n + 1)
                act.copy(parts[0:VROWS, n, part], small[:, n]).then_inc(part_cast[part], 1)

            for n, f in enumerate(LOOKED_UP):
                act.dma_start(small[:, n], tables[f - 1].rearrange("(c p) d -> p c d", p=VROWS)
                              ).then_inc(small_loaded[n], 16)
            act.dma_start(w2[:], W2.rearrange("(k p) n -> p k n", p=P)).then_inc(weights_loaded, 16)
            for tile, dram in ((w3, W3), (bias1, b1), (bias2, b2)):
                act.dma_start(tile[:], dram).then_inc(weights_loaded, 16)
            cast_part(0, 0)
            cast_part(1, 0)
            for n in range(NL):
                cast_part(n, 1)
                if n + 2 < NL:
                    cast_part(n + 2, 0)
                cast_part(n, 2)
                if n > 0:
                    place_lookup(0, n - 1)
            place_lookup(0, NL - 1)
            def move_gram(i, p, first):
                if p == 0 and not first:
                    act.wait_ge(z_packed, PACKED * i)
                for h in range(HALVES):
                    act.wait_ge(gram_done, HALVES * (2 * i + p) + h + 1)
                    for c in range(NQUAD):
                        s = P * p + (h * NQUAD + c) * PER_QUAD
                        ins = act.copy(gram[0:F, :, s:s + PER_QUAD],
                                       gram_ps[h][QUAD * c:QUAD * c + F, :, :].rearrange("f s g -> f g s"))
                    ins.then_inc(gram_moved, 1)

            def mlp(j, column, width=PAIR, first=False):
                for m in range(M1):
                    act.wait_ge(h1_done, M1 * j + m + 1)
                    if m == 0 and not first:
                        act.wait_ge(h2_done, M2 * j)
                    act.activation(h1[:, m, 0:width], mlp_ps[m % 2][:, 0:width], ACT.Relu,
                                   bias=bias1[:, m:m + 1]).then_inc(h1_ready, 1)
                for m in range(M2):
                    act.wait_ge(h2_done, M2 * j + m + 1)
                    if m == 0 and not first:
                        act.wait_ge(y_done, j)
                    act.activation(h2[:, m, 0:width], mlp_ps[m % 2][:, 0:width], ACT.Relu,
                                   bias=bias2[:, m:m + 1]).then_inc(h2_ready, 1)
                act.wait_ge(y_done, j + 1)
                if not first:
                    act.wait_ge(y_stored, 16 * j)
                act.copy(y[:, 0:width], y_ps[:, 0:width]).then_inc(y_ready, 1)
                act.wait_ge(y_ready, j + 1)
                act.dma_start(out[:, bass.ds(column, width)], y[:, 0:width]).then_inc(y_stored, 16)

            for p in range(2):
                move_gram(0, p, True)
            act.wait_ge(weights_loaded, 16 * WEIGHT_LOADS)
            place_lookups(1)
            move_gram(1, 0, False)
            mlp(0, 0, first=True)
            move_gram(1, 1, False)
            with act.Fori(2, LAST) as i:
                place_lookups(i)
                move_gram(i, 0, False)
                mlp(i - 1, PAIR * (i - 1))
                move_gram(i, 1, False)
            place_lookups(LAST)
            move_gram(LAST, 0, False)
            mlp(LAST - 1, PAIR * (LAST - 1))
            mlp(LAST, B - PAIR, P)
            move_gram(LAST, 1, False)
            mlp(LAST + 1, B - P, P)
            act.wait_ge(y_stored, 16 * (LAST + 2))


def kernel(**inputs):
    import concourse.bacc as bacc
    from concourse.bass_utils import run_bass_kernel_spmd

    nc = bacc.Bacc("TRN2", target_bir_lowering=False, num_devices=1)
    arrays = {}

    def dram(name, a):
        arrays[name] = np.ascontiguousarray(a)
        return nc.dram_tensor(name, arrays[name].shape, mybir.dt.from_np(arrays[name].dtype), kind="ExternalInput").ap()

    bottomT = dram("bottomT", np.asarray(inputs["r_bottom_output"]).T)
    ids = dram("ids", inputs["ids"])
    ids_rows = dram("ids_rows", np.asarray(inputs["ids"]).T[[f - 1 for f in LOOKED_UP]])
    tables = [dram(f"tbl_{n}", inputs[f"tbl_{n}"]) for n in range(NUM_TABLES)]
    W1 = dram("W1", inputs["W_top1"])
    b1 = dram("b1", np.asarray(inputs["b_top1"]).reshape(-1, P).T)
    W2 = dram("W2", inputs["W_top2"])
    b2 = dram("b2", np.asarray(inputs["b_top2"]).reshape(-1, P).T)
    W3 = dram("W3", np.asarray(inputs["W_top3"]).reshape(-1, P).T)
    B = arrays["ids"].shape[0]
    out = nc.dram_tensor("out", (1, B), F32, kind="ExternalOutput").ap()
    tower(nc, bottomT, ids, ids_rows, tables, W1, b1, W2, b2, W3, out)
    r = run_bass_kernel_spmd(nc, [arrays], core_ids=[0])
    return np.asarray(r.results[0]["out"]).reshape(B, 1)
```

```python
from contextlib import ExitStack

import numpy as np

import concourse.bass as bass
from concourse import mybir

ACT = mybir.ActivationFunctionType
ALU = mybir.AluOpType
F32 = mybir.dt.float32
F32R = mybir.dt.float32r
I32 = mybir.dt.int32

P = 128
NUM_TABLES = 26
F = NUM_TABLES + 1
LOOKED_UP = (8, 12, 17, 19, 20, 22, 24, 26)
GATHERED = [f for f in range(1, F) if f not in LOOKED_UP]
GROUP = 4
PARTS = 2


def evenly_spaced(features, most):
    runs = []
    for f in features:
        run = runs[-1] if runs else []
        if run and len(run) < most and (len(run) == 1 or f - run[-1] == run[-1] - run[-2]):
            run.append(f)
        else:
            runs.append([f])
    return runs


GROUPS = evenly_spaced(GATHERED, GROUP)
NG = len(GROUPS)
NL = len(LOOKED_UP)
SET = NL // 2
assert NL % 4 == 0
PLACES = []
for k in range(2):
    n, copies = SET * k, []
    for run in evenly_spaced(LOOKED_UP[SET * k:SET * (k + 1)], SET):
        copies.append((n, run))
        n += len(run)
    PLACES.append(copies)
NPLACES = sum(len(copies) for copies in PLACES)
QUAD = 32
NQUAD = P // QUAD
HALVES = 2
PER_QUAD = P // HALVES // NQUAD
PAIR = 2 * P
WIDE = 2 * PAIR

CHUNKS = 3

TRIPLES = []
ZROWS = 0
for t in range(0, F - 1, CHUNKS):
    TRIPLES.append((t, t + 1, ZROWS, F - 1 - t))
    ZROWS += F - 1 - t
assert ZROWS <= P
LAST_PACKS = {"sp": [x for n, x in enumerate(TRIPLES) if n % 3 < 2],
              "pool": [x for n, x in enumerate(TRIPLES) if n % 3 == 2]}


def tower(nc, bottomT, ids, ids_looked, tables, W1, b1, W2, b2, W3, out):
    B = bottomT.shape[1]
    TILES = B // P
    NPAIR_TILES = B // PAIR
    NWIDE = B // WIDE
    assert B % WIDE == 0
    H1, H2 = W1.shape[1], W2.shape[1]
    M1, M2 = H1 // P, H2 // P
    assert NG >= M1
    chunk_rows = [ZROWS] * CHUNKS + [P]
    NPAIRS = F * (F - 1) // 2
    V = tables[LOOKED_UP[0] - 1].shape[0]
    VCHUNKS = -(-V // P)
    VROWS = V // VCHUNKS
    assert VROWS * VCHUNKS == V and all(tables[f - 1].shape[0] == V for f in LOOKED_UP)
    HALF_CHUNKS = VCHUNKS // 2
    SMALL_SLOTS = F * PAIR // (VCHUNKS * P)
    assert VCHUNKS % 2 == 0
    PACKED = 16 * len(TRIPLES)

    with ExitStack() as ctx:
        def sb(name, shape, dt=F32):
            return ctx.enter_context(nc.sbuf_tensor(name, shape, dt))

        def sem(name):
            return ctx.enter_context(nc.semaphore(name))

        identity = sb("identity", [P, P])
        ids_all = sb("ids_all", [P, TILES, NUM_TABLES], I32)
        ids_now = [sb(f"ids_now{p}", [P, NUM_TABLES], I32) for p in range(2)]
        rows = [sb(f"rows{p}", [P, len(GATHERED), P]) for p in range(2)]
        embT = sb("embT", [P, PAIR, F])
        row_number_i = sb("row_number_i", [P, VCHUNKS], I32)
        row_number = sb("row_number", [P, VCHUNKS])
        ids_wide = sb("ids_wide", [P, SET, WIDE], I32)
        onehot = [sb(f"onehot{b}", [P, HALF_CHUNKS, WIDE], F32R) for b in range(2)]
        parts = sb("parts", [P, NL, PARTS, VCHUNKS, P], F32R)
        staged = sb("staged", [P, NL, WIDE])
        bottom = [sb(f"bottom{b}", [P, PAIR]) for b in range(2)]
        gram = sb("gram", [P, F, PAIR])
        small = gram[0:VROWS].rearrange("p f s -> p (f s)")[:, 0:SMALL_SLOTS * VCHUNKS * P].rearrange(
            "p (n c d) -> p n c d", n=SMALL_SLOTS, c=VCHUNKS)
        z = sb("z", [P, CHUNKS, PAIR])
        w1 = sb("w1", [P, CHUNKS + 1, H1])
        w2 = sb("w2", [P, M1, H2])
        w3 = sb("w3", [P, M2])
        bias1 = sb("bias1", [P, M1])
        bias2 = sb("bias2", [P, M2])
        h1 = sb("h1", [P, M1, PAIR])
        h2 = sb("h2", [P, M2, PAIR])
        y = sb("y", [1, PAIR])

        turned = [ctx.enter_context(nc.psum_tensor(f"turned{b}", [P, GROUP, P], F32)) for b in range(2)]
        gram_ps = [ctx.enter_context(nc.psum_tensor(f"gram_ps{h}", [P, PER_QUAD, F], F32)) for h in range(HALVES)]
        looked_ps = [ctx.enter_context(nc.psum_tensor(f"looked_ps{b}", [P, WIDE], F32)) for b in range(2)]
        mlp_ps = [ctx.enter_context(nc.psum_tensor(f"mlp_ps{b}", [P, 512], F32)) for b in range(2)]
        y_ps = mlp_ps[0][0:1, 0:PAIR]

        ids_loaded = sem("ids_loaded")
        bottom_loaded = sem("bottom_loaded")
        weights_loaded = sem("weights_loaded")
        identity_zero = sem("identity_zero")
        identity_ready = sem("identity_ready")
        first_ids_loaded = [sem(f"first_ids_loaded{t}") for t in range(2)]
        ids_staged = sem("ids_staged")
        tile_begun = sem("tile_begun")
        gathered = [[sem(f"gathered{p}_{g}") for g in range(NG)] for p in range(2)]
        group_turned = sem("group_turned")
        group_placed = sem("group_placed")
        bottom_placed = sem("bottom_placed")
        wide_loaded = [sem(f"wide_loaded{k}") for k in range(SET)]
        numbers_made = sem("numbers_made")
        numbers_ready = sem("numbers_ready")
        small_loaded = [sem(f"small_loaded{n}") for n in range(NL)]
        high_cast = sem("high_cast")
        low_cast = sem("low_cast")
        onehot_built = sem("onehot_built")
        looked_up = sem("looked_up")
        looked_staged = sem("looked_staged")
        lookup_placed = sem("lookup_placed")
        w1_zero = sem("w1_zero")
        gram_done = sem("gram_done")
        gram_moved = sem("gram_moved")
        last_moved = sem("last_moved")
        last_packed = {q: sem(f"last_packed_{q}") for q in LAST_PACKS}
        z_packed = sem("z_packed")
        h1_done = sem("h1_done")
        h1_ready = sem("h1_ready")
        h2_done = sem("h2_done")
        h2_ready = sem("h2_ready")
        y_done = sem("y_done")
        y_ready = sem("y_ready")
        y_stored = sem("y_stored")

        WEIGHT_LOADS = F - 1 + 1 + 4
        LAST = NPAIR_TILES - 1
        SMALL_BY_ACT = 2
        AHEAD = 2

        def halves_of(k):
            return [(n, half) for n in range(SET * k, SET * (k + 1)) for half in range(2)]

        def first_turns(n):
            p, slot = n // SET, n % SET
            return [(p, g) for g in range(NG) if 1 + g * (SET - 1) // NG == slot]

        block = ctx.enter_context(nc.Block())

        def move_gram_half(engine, copy, moved, i, p, h, quads):
            engine.wait_ge(gram_done, HALVES * (2 * i + p) + h + 1)
            for c in quads:
                s = P * p + (h * NQUAD + c) * PER_QUAD
                ins = copy(gram[0:F, :, s:s + PER_QUAD],
                           gram_ps[h][QUAD * c:QUAD * c + F, :, :].rearrange("f s g -> f g s"))
            ins.then_inc(moved, 1)

        def place_group(engine, copy, i, p, g):
            features = GROUPS[g]
            n = len(features)
            step = features[1] - features[0] if n > 1 else 1
            engine.wait_ge(group_turned, NG * (2 * i + p) + g + 1)
            copy(embT[:, P * p:P * p + P, features[0]:features[-1] + 1:step],
                 turned[(NG * p + g) % 2][:, 0:n, :].rearrange("p f s -> p s f")).then_inc(group_placed, 1)

        def pack_last(engine, queue):
            engine.wait_ge(h1_done, M1 * LAST)
            engine.wait_ge(last_moved, 2 * HALVES)
            for f, g, row, n in LAST_PACKS[queue]:
                engine.dma_start(z[row:row + n, :, P:PAIR], gram[g:g + n, f:f + CHUNKS, P:PAIR]
                                 ).then_inc(last_packed[queue], 16)

        def load_small(engine, n):
            engine.dma_start(small[:, n % SMALL_SLOTS], tables[LOOKED_UP[n] - 1].rearrange("(c p) d -> p c d", p=VROWS)
                             ).then_inc(small_loaded[n], 16)

        @block.sync
        def _(sp):
            def load_wide(q, n, first=False):
                if not (first and n < SET):
                    sp.wait_ge(onehot_built, 2 * (NL * q + n - SET + 1))
                sp.dma_start(ids_wide[:, n % SET, :],
                             ids_looked[0:1, bass.ds(WIDE * (NL * q + n), WIDE)].to_broadcast([P, WIDE])
                             ).then_inc(wide_loaded[n % SET], 16)

            def load_bottom(i, b):
                sp.dma_start(bottom[b][:], bottomT[:, bass.ds(PAIR * i, PAIR)]).then_inc(bottom_loaded, 16)

            def load_first_ids(t):
                sp.dma_start(ids_now[t][:], ids[P * t:P * (t + 1), :]).then_inc(first_ids_loaded[t], 16)

            load_first_ids(0)
            load_wide(0, 0, True)
            load_small(sp, SMALL_BY_ACT)
            for n in range(1, SET):
                load_wide(0, n, True)
            for n in range(SMALL_BY_ACT + 1, SMALL_SLOTS):
                load_small(sp, n)
            load_first_ids(1)
            sp.dma_start(ids_all[:], ids.rearrange("(t p) f -> p t f", p=P)).then_inc(ids_loaded, 16)
            for b in range(2):
                load_bottom(b, b)
            sp.wait_ge(w1_zero, 1)
            w1_row = 0
            for f in range(F - 1):
                first_f, first_g, row, n = TRIPLES[f // CHUNKS]
                row += f + 1 - first_g
                n = F - 1 - f
                sp.dma_start(w1[row:row + n, f - first_f, :], W1[w1_row:w1_row + n, :]).then_inc(weights_loaded, 16)
                w1_row += n
            sp.dma_start(w1[:, CHUNKS, :], W1[NPAIRS:NPAIRS + P, :]).then_inc(weights_loaded, 16)
            for n in range(SMALL_SLOTS, NL):
                sp.wait_ge(low_cast, n - SMALL_SLOTS + 1)
                load_small(sp, n)
            for n in range(SET, NL):
                load_wide(0, n, True)
            for n in range(SET):
                load_wide(1, n)

            def pack(j, moved, at=0, width=PAIR, b=None, first=False):
                if not first:
                    sp.wait_ge(h1_done, M1 * j)
                    if b is not None:
                        load_bottom(j + 1, b)
                sp.wait_ge(gram_moved, HALVES * moved)
                for f, g, row, n in TRIPLES:
                    sp.dma_start(z[row:row + n, :, at:at + width],
                                 gram[g:g + n, f:f + CHUNKS, at:at + width]).then_inc(z_packed, 16)

            pack(0, 2, first=True)
            for n in range(SET, NL):
                load_wide(1, n)
            with sp.Fori(2, NWIDE) as q:
                for k in range(2):
                    j = 2 * q - 3 + k
                    pack(j, 2 * j + 2, b=k)
                    for n in range(SET * k, SET * (k + 1)):
                        load_wide(q, n)
            for j in range(LAST - 2, LAST):
                pack(j, 2 * j + 2, b=(j + 1) % 2)
            pack(LAST, TILES - 1, 0, P)
            pack_last(sp, "sp")

        @block.gpsimd
        def _(pool):
            pool.memset(identity[:], 0.0).then_inc(identity_zero, 1)
            pool.wait_ge(identity_zero, 1)
            pool.affine_select(out=identity[:], in_=identity[:], compare_op=ALU.not_equal, fill=1.0, base=0,
                               pattern=[[-1, P]], channel_multiplier=1).then_inc(identity_ready, 1)

            pool.iota(row_number_i[:], pattern=[[VROWS, VCHUNKS]], base=0, channel_multiplier=1).then_inc(numbers_made, 1)
            pool.memset(w1[:, 0:CHUNKS, :], 0.0).then_inc(w1_zero, 1)

            def gather(i, p, first):
                if not first:
                    pool.wait_ge(group_turned, NG * (2 * i + p - 1))
                    pool.wait_ge(ids_staged, 2 * i + p - 1)
                else:
                    pool.wait_ge(first_ids_loaded[p], 16)
                pool.sem_inc(tile_begun, 1)
                for g, features in enumerate(GROUPS):
                    for f in features:
                        pool.indirect_dma_start(
                            rows[p][:, GATHERED.index(f), :], None, tables[f - 1],
                            bass.IndirectOffsetOnAxis(ap=ids_now[p][:, f - 1:f], axis=0),
                        ).then_inc(gathered[p][g], 16)

            for p in range(2):
                gather(0, p, True)
            with pool.Fori(1, NPAIR_TILES) as i:
                for p in range(2):
                    gather(i, p, False)
            pack_last(pool, "pool")

        @block.tensor
        def _(pe):
            def look_up(q, n, half, first=False):
                if first and half == 0:
                    pe.wait_ge(low_cast, n + 1)
                pe.wait_ge(onehot_built, 2 * (NL * q + n) + half + 1)
                if half == 0 and not (first and n < 2):
                    pe.wait_ge(looked_staged, NL * q + n - 1)
                for c in range(HALF_CHUNKS):
                    for part in range(PARTS):
                        mm = pe.matmul(looked_ps[n % 2][:], parts[0:VROWS, n, part, HALF_CHUNKS * half + c, :],
                                       onehot[half][0:VROWS, c, :], start=(half == 0 and c == 0 and part == 0),
                                       stop=(half == 1 and c == HALF_CHUNKS - 1 and part == PARTS - 1))
                mm.then_inc(looked_up, 1)

            def turn(i, p, g, first=False):
                b = (NG * p + g) % 2
                pe.wait_ge(gathered[p][g], 16 * len(GROUPS[g]) * (i + 1))
                if not (first and NG * p + g < 2):
                    pe.wait_ge(group_placed, NG * (2 * i + p) + g - 1)
                for k, f in enumerate(GROUPS[g]):
                    mm = pe.transpose(turned[b][:, k, :], rows[p][:, GATHERED.index(f), :], identity[:])
                mm.then_inc(group_turned, 1)

            def grams(i, p, h, first=False):
                pe.wait_ge(group_placed, NG * (2 * i + p + 1))
                pe.wait_ge(bottom_placed, i + 1)
                pe.wait_ge(lookup_placed, NPLACES * (i + 1))
                if not first:
                    pe.wait_ge(gram_moved, HALVES * (2 * i + p - 1) + h + 1)
                for q in range(PER_QUAD):
                    for c in range(NQUAD):
                        e = embT[:, P * p + (h * NQUAD + c) * PER_QUAD + q, :]
                        mm = pe.matmul(gram_ps[h][QUAD * c:QUAD * c + F, q, :], e, e, start=True, stop=True)
                mm.then_inc(gram_done, 1)

            def look_up_phase(i, q=None, k=None):
                halves = halves_of(k) if q is not None else []
                for m in range(max(len(halves), NG)):
                    if k == 0 and m < HALVES:
                        grams(i - 1, 1, m)
                    if m < len(halves):
                        look_up(q, *halves[m])
                    if k != 0 and m < HALVES:
                        grams(i - 1, 1, m)
                    if m < NG:
                        turn(i, 0, m)

            def mlp(j, b, width=PAIR, at=0, grams_of=None, turn_of=None, first=False, last=False):
                if last:
                    for q in LAST_PACKS:
                        pe.wait_ge(last_packed[q], 16 * len(LAST_PACKS[q]))
                else:
                    pe.wait_ge(z_packed, PACKED * (j + 1))
                for m in range(M1):
                    if m == 0 and not first:
                        pe.wait_ge(y_ready, j)
                    if m >= 2:
                        pe.wait_ge(h1_ready, M1 * j + m - 1)
                    for k, n in enumerate(chunk_rows):
                        x = z[0:n, k, at:at + width] if k < CHUNKS else bottom[b][:, at:at + width]
                        mm = pe.matmul(mlp_ps[m % 2][:, 0:width], w1[0:n, k, P * m:P * m + P], x,
                                       start=(k == 0), stop=(k == CHUNKS))
                    mm.then_inc(h1_done, 1)
                    if grams_of is not None and m < HALVES:
                        grams(grams_of, 0, m)
                    if turn_of is not None:
                        turn(turn_of, 1, m)
                for m in range(M2):
                    for k in range(M1):
                        if m == 0:
                            pe.wait_ge(h1_ready, M1 * j + max(k + 1, M1 - 1))
                        mm = pe.matmul(mlp_ps[m % 2][:, 0:width], w2[:, k, P * m:P * m + P], h1[:, k, 0:width],
                                       start=(k == 0), stop=(k == M1 - 1))
                    mm.then_inc(h2_done, 1)
                    if turn_of is not None:
                        for g in range(M1 + m, NG, M2):
                            turn(turn_of, 1, g)
                for k in range(M2):
                    pe.wait_ge(h2_ready, M2 * j + k + 1)
                    mm = pe.matmul(y_ps[:, 0:width], w3[:, k:k + 1], h2[:, k, 0:width], start=(k == 0), stop=(k == M2 - 1))
                mm.then_inc(y_done, 1)

            pe.wait_ge(identity_ready, 1)
            for n in range(NL):
                for half in range(2):
                    look_up(0, n, half, True)
                for p, g in first_turns(n):
                    turn(0, p, g, True)
            for h in range(HALVES):
                grams(0, 0, h, True)
            look_up_phase(1, 1, 0)
            pe.wait_ge(weights_loaded, 16 * WEIGHT_LOADS)
            mlp(0, 0, grams_of=1, turn_of=1, first=True)
            look_up_phase(2, 1, 1)
            mlp(1, 1, grams_of=2, turn_of=2)
            with pe.Fori(2, NWIDE) as q:
                for k in range(2):
                    i = 2 * q - 1 + k
                    look_up_phase(i, q, k)
                    mlp(i - 1, k, grams_of=i, turn_of=i)
            look_up_phase(LAST)
            for h in range(HALVES):
                grams(LAST, 0, h)
            mlp(LAST - 1, 0, turn_of=LAST)
            for h in range(HALVES):
                grams(LAST, 1, h)
            mlp(LAST, 1, P, 0)
            mlp(LAST + 1, 1, P, P, last=True)

        @block.vector
        def _(dve):
            def stage_ids(t, slot):
                dve.tensor_copy(ids_now[slot][:], ids_all[:, bass.ds(t, 1), :].rearrange("p a f -> p (a f)")).then_inc(ids_staged, 1)

            def build_onehot(q, n, half, first=False):
                dve.wait_ge(wide_loaded[n % SET], 16 * (2 * q + n // SET + 1))
                if not (first and n == 0):
                    dve.wait_ge(looked_up, 2 * (NL * q + n) + half - 1)
                for c in range(HALF_CHUNKS):
                    k = HALF_CHUNKS * half + c
                    ins = dve.tensor_scalar(onehot[half][:, c, :], ids_wide[:, n % SET, :],
                                            row_number[:, k:k + 1], None, ALU.is_equal)
                ins.then_inc(onehot_built, 1)

            def place_bottom(i, b, first=False):
                dve.wait_ge(bottom_loaded, 16 * (i + 1))
                if not first:
                    dve.wait_ge(gram_done, 2 * HALVES * i)
                dve.tensor_copy(embT[:, :, 0], bottom[b][:]).then_inc(bottom_placed, 1)

            def place(i, p, g):
                if g == 0:
                    dve.wait_ge(gram_done, HALVES * (2 * i + p - 1))
                place_group(dve, dve.tensor_copy, i, p, g)

            def cast_low(n):
                dve.wait_ge(high_cast, n + 1)
                dve.tensor_tensor(parts[0:VROWS, n, 1], small[:, n % SMALL_SLOTS], parts[0:VROWS, n, 0].bitcast(F32),
                                  ALU.subtract).then_inc(low_cast, 1)

            dve.wait_ge(numbers_made, 1)
            dve.tensor_copy(row_number[:], row_number_i[:]).then_inc(numbers_ready, 1)
            cast_low(0)
            dve.wait_ge(numbers_ready, 1)
            for n in range(NL):
                for half in range(2):
                    build_onehot(0, n, half, True)
                if n + 1 < NL:
                    cast_low(n + 1)
                if n == SET:
                    dve.wait_ge(ids_loaded, 16)
                    dve.wait_ge(group_turned, NG)
                    stage_ids(2, 0)
                    place_bottom(0, 0, True)
            dve.wait_ge(group_turned, 2 * NG)

            def turn_of_pair(i, b, q=None, k=None):
                stage_ids(2 * i + 1, 1)
                halves = halves_of(k) if q is not None else []
                if k == 0:
                    for half in halves[0:AHEAD]:
                        build_onehot(q, *half)
                for m in range(max(len(halves), NG)):
                    if m + AHEAD < len(halves):
                        build_onehot(q, *halves[m + AHEAD])
                    if m < NG:
                        place(i, 0, m)
                place_bottom(i, b)
                if q is not None:
                    stage_ids(2 * i + 2, 0)
                for g in range(NG):
                    place(i, 1, g)
                    if k == 0 and 2 <= g < 2 + AHEAD:
                        build_onehot(q, *halves_of(1)[g - 2])

            turn_of_pair(1, 1, 1, 0)
            turn_of_pair(2, 0, 1, 1)
            with dve.Fori(2, NWIDE) as q:
                for k in range(2):
                    turn_of_pair(2 * q - 1 + k, 1 - k, q, k)
            turn_of_pair(LAST, 1)
            for h in range(HALVES):
                move_gram_half(dve, dve.tensor_copy, last_moved, LAST, 1, h, range(NQUAD // 2, NQUAD))

        @block.scalar
        def _(act):
            def stage_lookup(q, n, first=False):
                if not first:
                    act.wait_ge(lookup_placed, 2 * NPLACES * q)
                act.wait_ge(looked_up, 2 * (NL * q + n + 1))
                act.copy(staged[:, n, :], looked_ps[n % 2][:]).then_inc(looked_staged, 1)

            def place_lookups(q, b, k):
                act.wait_ge(looked_staged, NL * q + SET * (k + 1))
                for n, features in PLACES[k]:
                    step = features[1] - features[0] if len(features) > 1 else 1
                    act.copy(embT[:, :, features[0]:features[-1] + 1:step],
                             staged[:, n:n + len(features), PAIR * b:PAIR * (b + 1)].rearrange("p n s -> p s n")
                             ).then_inc(lookup_placed, 1)

            def cast_high(n):
                act.wait_ge(small_loaded[n], 16)
                act.copy(parts[0:VROWS, n, 0], small[:, n % SMALL_SLOTS]).then_inc(high_cast, 1)

            for n in range(SMALL_BY_ACT):
                load_small(act, n)
            for n in range(2):
                cast_high(n)
            for n in range(NL):
                if n + 2 < NL:
                    cast_high(n + 2)
                stage_lookup(0, n, True)
                for p, g in first_turns(n):
                    place_group(act, act.copy, 0, p, g)
                if n % SET == SET - 1:
                    place_lookups(0, 0, n // SET)
            act.dma_start(w2[:], W2.rearrange("(k p) n -> p k n", p=P)).then_inc(weights_loaded, 16)
            for tile, dram in ((w3, W3), (bias1, b1), (bias2, b2)):
                act.dma_start(tile[:], dram).then_inc(weights_loaded, 16)

            def move_gram(i, p, h, first=False):
                if p == 0 and h == 0 and not first:
                    act.wait_ge(z_packed, PACKED * i)
                move_gram_half(act, act.copy, gram_moved, i, p, h, range(NQUAD))

            def mlp(j, column, width=PAIR, grams_of=None, first=False):
                for m in range(M1):
                    act.wait_ge(h1_done, M1 * j + m + 1)
                    if m == 0 and not first:
                        act.wait_ge(h2_done, M2 * j)
                    act.activation(h1[:, m, 0:width], mlp_ps[m % 2][:, 0:width], ACT.Relu,
                                   bias=bias1[:, m:m + 1]).then_inc(h1_ready, 1)
                    if grams_of is not None and m < HALVES:
                        move_gram(grams_of, 0, m)
                for m in range(M2):
                    act.wait_ge(h2_done, M2 * j + m + 1)
                    if m == 0 and not first:
                        act.wait_ge(y_done, j)
                    act.activation(h2[:, m, 0:width], mlp_ps[m % 2][:, 0:width], ACT.Relu,
                                   bias=bias2[:, m:m + 1]).then_inc(h2_ready, 1)
                act.wait_ge(y_done, j + 1)
                if not first:
                    act.wait_ge(y_stored, 16 * j)
                act.copy(y[:, 0:width], y_ps[:, 0:width]).then_inc(y_ready, 1)
                act.wait_ge(y_ready, j + 1)
                act.dma_start(out[:, bass.ds(column, width)], y[:, 0:width]).then_inc(y_stored, 16)

            def look_up_phase(i, q=None, k=None):
                for h in range(HALVES):
                    move_gram(i - 1, 1, h)
                if k == 1:
                    place_lookups(q, 0, 0)
                    for n in range(SET, NL):
                        stage_lookup(q, n)
                    place_lookups(q, 0, 1)
                else:
                    for m in range(2):
                        place_lookups(q - 1 if q is not None else NWIDE - 1, 1, m)
                    if q is not None:
                        for n in range(SET):
                            stage_lookup(q, n)

            for h in range(HALVES):
                move_gram(0, 0, h, True)
            look_up_phase(1, 1, 0)
            act.wait_ge(weights_loaded, 16 * WEIGHT_LOADS)
            mlp(0, 0, grams_of=1, first=True)
            look_up_phase(2, 1, 1)
            mlp(1, PAIR, grams_of=2)
            with act.Fori(2, NWIDE) as q:
                for k in range(2):
                    i = 2 * q - 1 + k
                    look_up_phase(i, q, k)
                    mlp(i - 1, PAIR * (i - 1), grams_of=i)
            look_up_phase(LAST)
            mlp(LAST - 1, PAIR * (LAST - 1), grams_of=LAST)
            for h in range(HALVES):
                move_gram_half(act, act.copy, last_moved, LAST, 1, h, range(0, NQUAD // 2))
            mlp(LAST, B - PAIR, P)
            mlp(LAST + 1, B - P, P)
            act.wait_ge(y_stored, 16 * (LAST + 2))


def kernel(**inputs):
    import concourse.bacc as bacc
    from concourse.bass_utils import run_bass_kernel_spmd

    nc = bacc.Bacc("TRN2", target_bir_lowering=False, num_devices=1)
    arrays = {}

    def dram(name, a):
        arrays[name] = np.ascontiguousarray(a)
        return nc.dram_tensor(name, arrays[name].shape, mybir.dt.from_np(arrays[name].dtype), kind="ExternalInput").ap()

    bottomT = dram("bottomT", np.asarray(inputs["r_bottom_output"]).T)
    ids = dram("ids", inputs["ids"])
    ids_looked = dram("ids_looked", np.asarray(inputs["ids"])[:, [f - 1 for f in LOOKED_UP]].reshape(
        -1, WIDE, NL).transpose(0, 2, 1).reshape(1, -1))
    tables = [dram(f"tbl_{n}", inputs[f"tbl_{n}"]) for n in range(NUM_TABLES)]
    W1 = dram("W1", inputs["W_top1"])
    b1 = dram("b1", np.asarray(inputs["b_top1"]).reshape(-1, P).T)
    W2 = dram("W2", inputs["W_top2"])
    b2 = dram("b2", np.asarray(inputs["b_top2"]).reshape(-1, P).T)
    W3 = dram("W3", np.asarray(inputs["W_top3"]).reshape(-1, P).T)
    B = arrays["ids"].shape[0]
    out = nc.dram_tensor("out", (1, B), F32, kind="ExternalOutput").ap()
    tower(nc, bottomT, ids, ids_looked, tables, W1, b1, W2, b2, W3, out)
    r = run_bass_kernel_spmd(nc, [arrays], core_ids=[0])
    return np.asarray(r.results[0]["out"]).reshape(B, 1)
```
